# Optimizing a Trainium2 kernel written in Bass

```python
import numpy as np
import jax
import jax.numpy as jnp

def _softmax(x, axis=-1):
    return jax.nn.softmax(x, axis=axis)
def _gelu(x):
    return jax.nn.gelu(x, approximate=True)
def _silu(x):
    return jax.nn.silu(x)
def _sigmoid(x):
    return jax.nn.sigmoid(x)
def _layernorm(x, axis=-1, eps=1e-5):
    m = jnp.mean(x, axis=axis, keepdims=True)
    v = jnp.var(x, axis=axis, keepdims=True)
    return (x - m) / jnp.sqrt(v + eps)
def _scatter_add(tgt, idx, src, axis=0):
    return tgt.at[idx].add(src)
def _segment_sum(src, seg, n):
    return jax.ops.segment_sum(src, seg, n)

kernel_name = 'mk_adj_preln_d2_adj_512_a7edea'

def setup_inputs(seed: int = 0):
    np.random.seed(seed)
    _w = jnp.asarray
    def _rec_inputs():
        import jax
        import jax.numpy as jnp
        _gk = jax.random.key(seed)
        x = -0.0005207 + 1.001 * jax.random.normal(jax.random.fold_in(_gk, 1), (4096, 512), jnp.float32)
        _a = jax.random.bernoulli(jax.random.fold_in(_gk, 2), 0.000976562, (4096, 4096))
        _a = jnp.logical_or(_a, jnp.swapaxes(_a, -1, -2))
        _a = jnp.logical_or(_a, jnp.eye(4096, dtype=bool))
        adj = _a.astype(jnp.int32)
        return x, adj
    x, adj = _rec_inputs()
    def _L0_gnn_setup():
        import jax, jax.numpy as jnp
        import numpy as np
        HEAD_SIZE = 8
        QK_DIM = 512
        V_DIM = 512
        N = 4096
        ATT_DIM = QK_DIM // HEAD_SIZE
        SCALE = ATT_DIM ** (-0.5)
        NEG_FILL = jnp.float32(-9000000000000000.0)
        key = jax.random.key(seed)
        k1, k2, k3, k4 = jax.random.split(key, 4)
        x1 = jax.random.normal(k1, (N, QK_DIM), dtype=jnp.float32)
        x2 = jax.random.normal(k2, (N, QK_DIM), dtype=jnp.float32)
        v = jax.random.normal(k3, (N, V_DIM), dtype=jnp.float32)
        adj = jax.random.randint(k4, (N, N), 0, 2, dtype=jnp.int32)
        return {'x1': x1, 'x2': x2, 'v': v, 'adj': adj}
    _L0_gnn_all = _L0_gnn_setup()
    _L0_gnn_in = {k: v for k, v in _L0_gnn_all.items() if k in ('x2', 'v', )}
    del _L0_gnn_all

    def _L1_gnn_setup():
        import jax, jax.numpy as jnp
        import numpy as np
        key = jax.random.key(seed)
        kX, kA, k1, k2, k3, k4 = jax.random.split(key, 6)
        N, Cin, Cout = (8192, 512, 512)
        X = jax.random.normal(kX, (N, Cin), dtype=jnp.float32)
        A = jax.random.randint(kA, (N, N), 0, 2, dtype=jnp.int32)
        bound = 1.0 / np.sqrt(Cin)
        W_nb = jax.random.uniform(k1, (Cout, Cin), jnp.float32, -bound, bound)
        b_nb = jax.random.uniform(k2, (Cout,), jnp.float32, -bound, bound)
        W_line = jax.random.uniform(k3, (Cout, Cin), jnp.float32, -bound, bound)
        b_line = jax.random.uniform(k4, (Cout,), jnp.float32, -bound, bound)
        return {'X': X, 'A': A, 'W_nb': W_nb, 'b_nb': b_nb, 'W_line': W_line, 'b_line': b_line, 'neibor_num': 64}
    _L1_gnn_all = _L1_gnn_setup()
    _L1_gnn_in = {k: v for k, v in _L1_gnn_all.items() if k in ('W_nb', 'b_nb', 'W_line', 'b_line', )}
    del _L1_gnn_all

    return {
        "x": x,
        "adj": adj,
        "L0_gnn_x2": _L0_gnn_in["x2"],
        "L0_gnn_v": _L0_gnn_in["v"],
        "L1_gnn_W_nb": _L1_gnn_in["W_nb"],
        "L1_gnn_b_nb": _L1_gnn_in["b_nb"],
        "L1_gnn_W_line": _L1_gnn_in["W_line"],
        "L1_gnn_b_line": _L1_gnn_in["b_line"],
    }

def reference(x, adj, L0_gnn_x2, L0_gnn_v, L1_gnn_W_nb, L1_gnn_b_nb, L1_gnn_W_line, L1_gnn_b_line):
    import jax
    import jax.numpy as jnp
    def _L0_gnn_ref(x1, x2, v, adj):
        import jax, jax.numpy as jnp
        import numpy as np
        HEAD_SIZE = 8
        QK_DIM = 512
        V_DIM = 512
        N = 4096
        ATT_DIM = QK_DIM // HEAD_SIZE
        SCALE = ATT_DIM ** (-0.5)
        NEG_FILL = jnp.float32(-9000000000000000.0)
        n = x1.shape[0]
        q = x1.reshape(n, HEAD_SIZE, -1).transpose(1, 0, 2) * SCALE
        k = x2.reshape(n, HEAD_SIZE, -1).transpose(1, 0, 2)
        vv = v.reshape(n, HEAD_SIZE, -1).transpose(1, 0, 2)
        scores = jnp.einsum('hnd,hmd->hnm', q, k)
        scores = jnp.where(adj > 0, scores, NEG_FILL)
        attn = jax.nn.softmax(scores, axis=-1)
        out = jnp.einsum('hnm,hmd->hnd', attn, vv)
        return out.transpose(1, 0, 2).reshape(n, -1)

    def _L1_gnn_ref(X, A, W_nb, b_nb, W_line, b_line, neibor_num):
        import jax, jax.numpy as jnp
        import numpy as np
        Ab = A > 0
        keep = Ab & (jnp.cumsum(Ab.astype(jnp.int32), axis=1) <= neibor_num)
        cnt = keep.sum(axis=1, keepdims=True).astype(X.dtype)
        nb_sum = keep.astype(X.dtype) @ X
        nb_mean = nb_sum / jnp.maximum(cnt, 1.0)
        xj = jax.nn.leaky_relu(nb_mean @ W_nb.T + b_nb)
        xi = jax.nn.leaky_relu(X @ W_line.T + b_line)
        return xi + jnp.where(cnt > 0, xj, jnp.zeros((), X.dtype))

    h = jnp.maximum(_layernorm(x, axis=-1), 0.0)
    x = x + _L0_gnn_ref(h, L0_gnn_x2, L0_gnn_v, adj)
    h = jnp.maximum(_layernorm(x, axis=-1), 0.0)
    x = x + _L1_gnn_ref(h, adj, L1_gnn_W_nb, L1_gnn_b_nb, L1_gnn_W_line, L1_gnn_b_line, 64)
    return x


_drawn_inputs = setup_inputs


def setup_inputs(seed=0):
    import zlib

    import numpy as np

    out = dict(_drawn_inputs(seed))
    spreads = {}
    factors = {'L1_gnn_b_nb': 4.564, 'L1_gnn_b_line': 4.055}
    for name, (base, spread) in spreads.items():
        noise = np.random.default_rng([zlib.crc32(name.encode()), seed]).standard_normal(out[name].shape)
        drawn = base * np.exp(spread * noise) if base else spread * noise
        out[name] = jnp.asarray(drawn.astype(out[name].dtype))
    for name, factor in factors.items():
        out[name] = (out[name] * factor).astype(out[name].dtype)
    return out
```

```python
from contextlib import ExitStack

import numpy as np
import concourse.bass as bass
from concourse import mybir

F32 = mybir.dt.float32
FR = mybir.dt.float32r
BF16 = mybir.dt.bfloat16
I32 = mybir.dt.int32
ALU = mybir.AluOpType
ACT = mybir.ActivationFunctionType
AX = mybir.AxisListType

P = 128
N = 4096
D = 512
H = 8
DH = D // H
NB = N // P
RB = 2
ROWS = RB * P
CW = 512
CPB = N // CW
CPS = RB * CPB
STEPS = H * N // ROWS
SPH = STEPS // H
PAIRS = STEPS // 2
UPS = N // ROWS
PIECES = 4
PW = N // PIECES
EV = 4
T_LAG = CPS + 3
V_LAG = T_LAG + 2
NEG = -9000000000000000.0
LOWEST = -3.0e38
EPS = 1e-5
KEEP = 64
PRE_MASKS = 12
KC = 8
assert UPS == CPS and UPS % EV == 0


def ge(eng, sem, value):
    if not isinstance(value, int) or value > 0:
        eng.wait_ge(sem, value)


def passed(eng, sem):
    eng.sem_inc(sem, 1)


def build(nc, x, adj, x2t, v, wnb_t, bnb, wline_t, bline, out):
    q_scr = nc.dram_tensor("q_scr", (H * NB, P, 2 * P), F32).ap()
    mask_scr = nc.dram_tensor("mask_scr", (NB, P, N), BF16).ap()
    att_scr = nc.dram_tensor("att_scr", (STEPS, P, RB, DH), F32).ap()
    acc_scr = nc.dram_tensor("acc_scr", (NB, P, D), F32).ap()
    with ExitStack() as ctx:
        common = shared_tensors(nc, ctx)
        with ExitStack() as phase:
            attention_inputs(nc, phase, common, x, adj, x2t, v, q_scr, mask_scr)
        with ExitStack() as phase:
            attention(nc, phase, common, adj, x2t, v, q_scr, mask_scr, att_scr)
    with ExitStack() as phase:
        aggregate(nc, phase, x, adj, wnb_t, bnb, wline_t, bline, att_scr, acc_scr, out)


class Tensors:
    pass


def shared_tensors(nc, ctx):
    c = Tensors()

    def sb(name, shape, dt):
        return ctx.enter_context(nc.sbuf_tensor(name, shape, dt))

    def sem(name):
        return ctx.enter_context(nc.semaphore(name))

    c.k_st = sb("k_st", [P, N], FR)
    c.v_st = sb("v_st", [P, NB, P], FR)
    c.k_raw = sb("k_raw", [P, 2, N // KC], F32)
    c.v_raw = sb("v_raw", [P, 2, NB // KC, DH], F32)
    c.adj_raw = sb("adj_raw", [P, 2, N // 2], I32)
    c.mask_stage = sb("mask_stage", [P, 2, N // 2], BF16)
    c.ident = sb("ident", [P, P], F32)
    c.fold = sb("fold", [P, P], F32)
    c.s_ident = sem("s_ident")
    c.s_kraw = [sem(f"s_kraw{b}") for b in range(2)]
    c.s_vraw = [sem(f"s_vraw{b}") for b in range(2)]
    c.s_ksplit = sem("s_ksplit")
    c.s_vsplit = sem("s_vsplit")
    c.s_khi = sem("s_khi")
    c.s_vhi = sem("s_vhi")
    c.s_adj = [sem(f"s_adj{b}") for b in range(2)]
    c.s_conv = sem("s_conv")
    c.s_mask = [sem(f"s_mask{b}") for b in range(2)]
    c.s_passed = sem("s_pool_passed")
    c.s_qk = sem("s_qk")
    c.s_pv = sem("s_pv")
    return c


def key_parts(pool, c, x2t, h, n0, free=None):
    w = N // KC

    def load(q):
        ge(pool, c.s_ksplit, n0 + q - 1)
        for half in range(2):
            pool.dma_start(c.k_raw[half * DH:(half + 1) * DH, q % 2, :],
                           x2t[bass.ds(h * DH, DH), q * w:(q + 1) * w]).then_inc(c.s_kraw[q % 2], 16)

    load(0)
    for q in range(KC):
        cols = slice(q * w, (q + 1) * w)
        if q + 1 < KC:
            load(q + 1)
        if free is not None:
            pool.wait_ge(c.s_qk, free + q + 1)
        pool.wait_ge(c.s_kraw[q % 2], 16 * n0 + 32 * (q // 2) + 32)
        ge(pool, c.s_ksplit, n0 + q)
        passed(pool, c.s_passed)
        pool.tensor_copy(c.k_st[:, cols], c.k_raw[:, q % 2, :]).then_inc(c.s_khi, 1)
        pool.wait_ge(c.s_khi, n0 + q + 1)
        pool.tensor_tensor(c.k_st[DH:, cols], c.k_raw[DH:, q % 2, :], c.k_st[DH:, cols].bitcast(F32),
                           ALU.subtract).then_inc(c.s_ksplit, 1)


def value_parts(pool, c, v, h, n0, free=None):
    w = NB // KC
    rows = v.rearrange("(t p) c -> p t c", p=P)

    def load(q):
        ge(pool, c.s_vsplit, n0 + q - 1)
        pool.dma_start(c.v_raw[:, q % 2], rows[:, q * w:(q + 1) * w, bass.ds(h * DH, DH)])\
            .then_inc(c.s_vraw[q % 2], 16)

    load(0)
    pool.wait_ge(c.s_ksplit, n0 + KC)
    for q in range(KC):
        blocks = slice(q * w, (q + 1) * w)
        if q + 1 < KC:
            load(q + 1)
        if free is not None:
            pool.wait_ge(c.s_pv, free + 2 * q + 2)
        pool.wait_ge(c.s_vraw[q % 2], 8 * n0 + 16 * (q // 2) + 16)
        passed(pool, c.s_passed)
        pool.tensor_copy(c.v_st[:, blocks, 0:DH], c.v_raw[:, q % 2]).then_inc(c.s_vhi, 1)
        pool.wait_ge(c.s_vhi, n0 + q + 1)
        pool.tensor_tensor(c.v_st[:, blocks, DH:], c.v_raw[:, q % 2], c.v_st[:, blocks, 0:DH].bitcast(F32),
                           ALU.subtract).then_inc(c.s_vsplit, 1)


def mask_block(pool, c, adj, mask_scr, t):
    w = N // 2
    for b in range(2):
        cols = slice(b * w, b * w + w)
        pool.dma_start(c.adj_raw[:, b, :], adj[bass.ds(t * P, P), cols]).then_inc(c.s_adj[b], 16)
    for b in range(2):
        cols = slice(b * w, b * w + w)
        pool.wait_ge(c.s_adj[b], 16 * t + 16)
        ge(pool, c.s_mask[b], 16 * t)
        passed(pool, c.s_passed)
        pool.tensor_scalar(c.mask_stage[:, b, :], c.adj_raw[:, b, :], 0, NEG, ALU.is_le, ALU.mult)\
            .then_inc(c.s_conv, 1)
        pool.wait_ge(c.s_conv, 2 * t + b + 1)
        pool.dma_start(mask_scr[t, :, cols] if isinstance(t, int) else
                       mask_scr[bass.ds(t, 1), :, cols].rearrange("o p n -> (o p) n"),
                       c.mask_stage[:, b, :]).then_inc(c.s_mask[b], 16)


def attention_inputs(nc, ctx, c, x, adj, x2t, v, q_scr, mask_scr):
    def sb(name, shape, dt):
        return ctx.enter_context(nc.sbuf_tensor(name, shape, dt))

    def sem(name):
        return ctx.enter_context(nc.semaphore(name))

    LG = 4
    xs = sb("xs", [P, NB, D], F32)
    stats = sb("stats", [P, NB, 6], F32)
    mv = sb("mv", [P, NB, 2], F32)
    ln = sb("ln", [P, 7, NB], F32)
    var, std, rstd, tmp, tmp2, scale, shift = (ln[:, i, :] for i in range(7))
    hd = sb("hd", [P, 2, H, 2, DH], F32)
    q_stage = sb("q_stage", [P, 2, H, 2, P], FR)
    pt = ctx.enter_context(nc.psum_tensor("pt", [P, 2, H, P], F32))
    s_x = [sem(f"s_x{g}") for g in range(LG)]
    s_stats, s_var, s_std, s_ln, s_scale, s_h, s_ht, s_hi, s_lo = (sem(f"s_p_{n}") for n in (
        "stats", "var", "std", "ln", "scale", "h", "ht", "hi", "lo"))
    s_q = [sem(f"s_q{b}") for b in range(2)]

    with nc.Block() as block:
        @block.sync
        def _(sp):
            rows = x.rearrange("(g t p) c -> g p t c", g=LG, p=P)
            for g in range(LG):
                w = NB // LG
                sp.dma_start(xs[:, g * w:(g + 1) * w, :], rows[g]).then_inc(s_x[g], 16)
            dst = q_scr.rearrange("(h t) p n -> t p h n", h=H)
            with sp.Fori(0, NB // 2) as i:
                for b in range(2):
                    sp.wait_ge(s_lo, 2 * i + b + 1)
                    sp.dma_start(dst[bass.ds(2 * i + b, 1)].rearrange("o p h n -> (o p) h n"),
                                 q_stage[:, b].rearrange("p h s n -> p h (s n)").bitcast(F32))\
                        .then_inc(s_q[b], 16)
            for b in range(2):
                sp.wait_ge(s_q[b], 16 * (NB // 2))

        @block.vector
        def _(dve):
            for t in range(NB):
                if t % (NB // LG) == 0:
                    dve.wait_ge(s_x[t // (NB // LG)], 16)
                dve.bn_stats(stats[:, t, :], xs[:, t, :]).then_inc(s_stats, 1)
            for t in range(NB):
                dve.wait_ge(s_stats, t + 1)
                dve.bn_aggr(mv[:, t, :], stats[:, t, :]).then_inc(s_ln, 1)
            dve.wait_ge(s_ln, NB)
            dve.tensor_scalar(var, mv[:, :, 1], EPS, None, ALU.add).then_inc(s_var, 1)
            dve.wait_ge(s_std, 1)
            refine_rstd(dve, var, std, rstd, tmp, tmp2, s_ln, NB)
            dve.tensor_scalar(scale, rstd, DH ** -0.5, None, ALU.mult).then_inc(s_ln, 1)
            dve.wait_ge(s_ln, NB + 6)
            dve.scalar_tensor_tensor(shift, mv[:, :, 0], -1.0, scale, ALU.mult, ALU.mult).then_inc(s_scale, 1)
            with dve.Fori(0, NB // 2) as i:
                for b in range(2):
                    dve.wait_ge(s_hi, 2 * i + b + 1)
                    dve.tensor_tensor(q_stage[:, b, :, 1, :], pt[:, b], q_stage[:, b, :, 0, :].bitcast(F32),
                                      ALU.subtract).then_inc(s_lo, 1)

        @block.scalar
        def _(act):
            act.wait_ge(s_var, 1)
            act.activation(std, var, ACT.Sqrt).then_inc(s_std, 1)
            act.wait_ge(s_scale, 1)

            def rounded(t, b):
                act.wait_ge(s_ht, t + 1)
                ge(act, s_q[b], 16 * ((t >> 1) if not isinstance(t, int) else t // 2))
                act.activation(q_stage[:, b, :, 0, :], pt[:, b], ACT.Copy).then_inc(s_hi, 1)

            for t in range(NB):
                b = t % 2
                if t >= 2:
                    act.wait_ge(s_ht, t - 1)
                src = xs[:, t, :].rearrange("p (h d) -> p h d", h=H).unsqueeze(2).to_broadcast([P, H, 2, DH])
                act.activation(hd[:, b], src, ACT.Relu, bias=shift[:, t:t + 1], scale=scale[:, t:t + 1])\
                    .then_inc(s_h, 1)
                if t >= 1:
                    rounded(t - 1, 1 - b)
            rounded(NB - 1, 1)

        @block.tensor
        def _(pe):
            pe.wait_ge(c.s_ident, 2)

            def transpose(t, b):
                pe.wait_ge(s_h, t + 1)
                ge(pe, s_lo, t - 1)
                for h in range(H):
                    last = pe.matmul(pt[:, b, h, :], hd[:, b, h].rearrange("p s d -> p (s d)"),
                                     c.ident[:, :], is_transpose=True, start=True, stop=True)
                last.then_inc(s_ht, 1)

            for b in range(2):
                transpose(b, b)
            with pe.Fori(1, NB // 2) as i:
                for b in range(2):
                    transpose(2 * i + b, b)

        @block.gpsimd
        def _(pool):
            pool.memset(c.ident[:, :], 0.0).then_inc(c.s_ident, 1)
            pool.wait_ge(c.s_ident, 1)
            pool.affine_select(out=c.ident[:, :], in_=c.ident[:, :], compare_op=ALU.not_equal, fill=1.0,
                               base=0, pattern=[[-1, P]], channel_multiplier=1).then_inc(c.s_ident, 1)
            pool.memset(c.fold[:, :], 0.0).then_inc(c.s_ident, 1)
            for n, base in enumerate((0, DH, -DH)):
                pool.wait_ge(c.s_ident, 3 + n)
                pool.affine_select(out=c.fold[:, :], in_=c.fold[:, :], compare_op=ALU.not_equal, fill=1.0,
                                   base=base, pattern=[[-1, P]], channel_multiplier=1).then_inc(c.s_ident, 1)
            key_parts(pool, c, x2t, 0, 0)
            value_parts(pool, c, v, 0, 0)
            mask_block(pool, c, adj, mask_scr, 0)
            with pool.Fori(1, PRE_MASKS) as t:
                mask_block(pool, c, adj, mask_scr, t)


def refine_rstd(dve, var, std, rstd, tmp, tmp2, s, count):
    def link(k):
        dve.wait_ge(s, count + k)
    dve.reciprocal(rstd, std).then_inc(s, 1)
    link(1)
    dve.tensor_tensor(tmp, rstd, rstd, ALU.mult).then_inc(s, 1)
    link(2)
    dve.tensor_tensor(tmp2, tmp, var, ALU.mult).then_inc(s, 1)
    link(3)
    dve.tensor_scalar(tmp, tmp2, -0.5, 1.5, ALU.mult, ALU.add).then_inc(s, 1)
    link(4)
    dve.tensor_tensor(rstd, rstd, tmp, ALU.mult).then_inc(s, 1)
    link(5)


def attention(nc, ctx, c, adj, x2t, v, q_scr, mask_scr, att_scr):
    def sb(name, shape, dt):
        return ctx.enter_context(nc.sbuf_tensor(name, shape, dt))

    def psum(name, shape):
        return ctx.enter_context(nc.psum_tensor(name, shape, F32))

    def sem(name):
        return ctx.enter_context(nc.semaphore(name))

    pr = [[sb(f"pr{a}{b}", [P, N], F32) for b in range(RB)] for a in range(2)]
    mask = [[sb(f"mask{a}{b}", [P, N], BF16) for b in range(RB)] for a in range(2)]
    q_st = sb("q_st", [P, 2, RB, 2, P], FR)
    pt_hi = sb("pt_hi", [P, EV, 2, ROWS], FR)
    pt_lo = sb("pt_lo", [P, EV, 2, ROWS], FR)
    o_sb = sb("o_sb", [P, 2, ROWS], F32)
    att_sb = sb("att_sb", [P, 2, RB, DH], F32)
    cmax = sb("cmax", [P, 2, RB, CPB], F32)
    nmax = sb("nmax", [P, 2, RB], F32)
    rsum = sb("rsum", [P, 2, RB, PIECES], F32)
    den = sb("den", [P, 2, RB], F32)
    rden = sb("rden", [P, 2, RB], F32)

    SBK = 4
    ps = psum("ps", [P, SBK, CW])
    pt = psum("pt2", [P, 2, 2, ROWS])
    po = psum("po", [P, 2, CW])

    s_qk, s_pv = c.s_qk, c.s_pv
    s_msk, s_max, s_exp, s_t, s_hi, s_lo, s_o, s_fold, s_den, s_rden, s_att = (
        sem(f"s_{n}") for n in ("msk", "max", "exp", "t", "hi", "lo", "o", "fold", "den", "rden", "att"))
    s_qld = [sem(f"s_qld{a}") for a in range(2)]
    s_mld = [[sem(f"s_mld{a}{b}") for b in range(RB)] for a in range(2)]
    s_st = [sem(f"s_st{a}") for a in range(2)]
    s_passed, s_sp_passed = sem("s_dve_passed"), sem("s_sp_passed")
    SLOTS = 2 * CPS

    def part(p, i, lag):
        n = SLOTS * p + i - lag
        there = not isinstance(p, int) or 0 <= n < STEPS * UPS
        g = (i - lag) % SLOTS
        return n, g // UPS, g % UPS, g, there

    def slots(eng, slot):
        for i in range(SLOTS):
            slot(0, i)
        with eng.Fori(1, PAIRS) as p:
            for i in range(SLOTS):
                slot(p, i)
        for i in range(V_LAG + 4):
            slot(PAIRS, i)

    with nc.Block() as block:
        @block.tensor
        def _(pe):
            def slot(p, i):
                n, a, k, g, there = part(p, i, 0)
                if there:
                    b, ck = k // CPB, k % CPB
                    if k == 0:
                        pe.wait_ge(s_qld[a], 16 * p + 16)
                    if a == 0 and b == 0:
                        pe.wait_ge(c.s_ksplit, KC * (p >> 3 if not isinstance(p, int) else p // 8) + ck + 1)
                    ge(pe, s_msk, n - SBK + 1)
                    for half in range(2):
                        last = pe.matmul(ps[:, g % SBK, :], q_st[:, a, b, half, :],
                                         c.k_st[:, ck * CW:(ck + 1) * CW], start=half == 0, stop=half == 1)
                    last.then_inc(s_qk, 1)
                n, a, u, g, there = part(p, i, T_LAG)
                if there:
                    if u % (UPS // PIECES) == 0:
                        pe.wait_ge(s_exp, exp_count(p, i, T_LAG, u // (UPS // PIECES)))
                    ge(pe, s_lo, n - 1)
                    for m in range(2):
                        for b in range(RB):
                            last = pe.matmul(pt[:, g % 2, m, b * P:(b + 1) * P],
                                             pr[a][b][:, (2 * u + m) * P:(2 * u + m + 1) * P],
                                             c.ident[:, :], is_transpose=True, start=True, stop=True)
                    last.then_inc(s_t, 1)
                n, a, u, g, there = part(p, i, V_LAG)
                if there:
                    e = g % EV
                    if u == 0:
                        ge(pe, s_att, step_count(p, i, V_LAG) - 1)
                    if a == 0 and u % 2 == 0:
                        hn = (p >> 3) if not isinstance(p, int) else p // 8
                        if i < V_LAG:
                            hn = ((p - 1) >> 3) if not isinstance(p, int) else (p - 1) // 8
                        pe.wait_ge(c.s_vsplit, KC * hn + u // 2 + 1)
                    pe.wait_ge(s_lo, n + 1)
                    for m in range(2):
                        for s, src in enumerate((pt_hi, pt_lo)):
                            last = pe.matmul(po[:, a, 0:ROWS], c.v_st[:, 2 * u + m, :], src[:, e, m, :],
                                             start=(u == 0 and m == 0 and s == 0),
                                             stop=(u == UPS - 1 and m == 1 and s == 1))
                    last.then_inc(s_pv, 1)
                if i % CPS == 7:
                    s, a, there = finished(p, i, 2)
                    if there:
                        pe.wait_ge(s_o, s + 1)
                        for b in range(RB):
                            last = pe.matmul(po[:, a, b * P:(b + 1) * P], o_sb[:, a, b * P:(b + 1) * P],
                                             c.fold[:, :], start=True, stop=True)
                        last.then_inc(s_fold, 1)
            slots(pe, slot)

        @block.vector
        def _(dve):
            def slot(p, i):
                n, a, k, g, there = part(p, i, 0)
                if there:
                    b, ck = k // CPB, k % CPB
                    if ck == 0:
                        dve.wait_ge(s_mld[a][b], 16 * p + 16)
                    ge(dve, s_t, SLOTS * (p - 1) + UPS * a + 2 * ck + 2)
                    dve.wait_ge(s_qk, n + 1)
                    passed(dve, s_passed)
                    cols = slice(ck * CW, (ck + 1) * CW)
                    masked(dve, pr[a][b][:, cols], ps[:, g % SBK, :], mask[a][b][:, cols],
                           cmax[:, a, b, ck:ck + 1]).then_inc(s_msk, 1)
                    if ck == CPB - 1:
                        dve.wait_ge(s_msk, n + 1)
                        dve.tensor_reduce(nmax[:, a, b:b + 1], cmax[:, a, b, :], AX.X, ALU.max, negate=True)\
                            .then_inc(s_max, 1)
                if i % CPS == 10:
                    s, a, there = finished(p, i, 1)
                    if there:
                        dve.wait_ge(s_exp, 2 * PIECES * (s + 1))
                        dve.tensor_reduce(den[:, a, :], rsum[:, a], AX.X, ALU.add).then_inc(s_den, 1)
                        dve.wait_ge(s_den, s + 1)
                        dve.reciprocal(rden[:, a, :], den[:, a, :]).then_inc(s_rden, 1)
                n, a, u, g, there = part(p, i, T_LAG)
                if there:
                    e = g % EV
                    dve.wait_ge(s_hi, n + 1)
                    dve.tensor_tensor(pt_lo[:, e], pt[:, g % 2], pt_hi[:, e].bitcast(F32), ALU.subtract)\
                        .then_inc(s_lo, 1)
            slots(dve, slot)

        @block.scalar
        def _(act):
            def slot(p, i):
                n, a, u, g, there = part(p, i, T_LAG)
                if there:
                    e = g % EV
                    act.wait_ge(s_t, n + 1)
                    ge(act, s_pv, n - EV + 1)
                    act.activation(pt_hi[:, e], pt[:, g % 2], ACT.Copy).then_inc(s_hi, 1)
                if i % 2 == 1:
                    b = 0 if i % CPS > 8 else 1
                    piece = (i % CPS - (9 if b == 0 else 1)) // 2
                    s, a, there = finished(p, i, b)
                    if there:
                        act.wait_ge(s_max, RB * s + b + 1)
                        cols = slice(piece * PW, (piece + 1) * PW)
                        act.activation(pr[a][b][:, cols], pr[a][b][:, cols], ACT.Exp, bias=nmax[:, a, b:b + 1],
                                       accum_out=rsum[:, a, b, piece:piece + 1]).then_inc(s_exp, 1)
                if i % CPS == 5:
                    s, a, there = finished(p, i, 2)
                    if there:
                        act.wait_ge(s_pv, UPS * (s + 1))
                        act.activation(o_sb[:, a, :], po[:, a, 0:ROWS], ACT.Copy).then_inc(s_o, 1)
                if i % CPS == 8:
                    s, a, there = finished(p, i, 2)
                    if there:
                        act.wait_ge(s_fold, s + 1)
                        act.wait_ge(s_rden, s + 1)
                        ge(act, s_st[a], 16 * p)
                        for b in range(RB):
                            last = act.activation(att_sb[:, a, b, :], po[:, a, b * P:b * P + DH], ACT.Copy,
                                                  scale=rden[:, a, b:b + 1])
                        last.then_inc(s_att, 1)
            act.sem_inc(s_att, 1)
            slots(act, slot)

        @block.sync
        def _(sp):
            for a in range(2):
                sp.sem_inc(s_st[a], 16)

            def load_mask(a, b, t):
                sp.dma_start(mask[a][b][:, :], mask_scr[bass.ds(t, 1)].rearrange("o p n -> (o p) n"))\
                    .then_inc(s_mld[a][b], 16)

            def load_q(a, s):
                sp.dma_start(q_st[:, a].bitcast(F32), q_scr[bass.ds(s * RB, RB)].rearrange("b p n -> p b n"))\
                    .then_inc(s_qld[a], 16)

            def store(a, s):
                sp.wait_ge(s_att, s + 2)
                sp.dma_start(att_scr[bass.ds(s, 1)].rearrange("o p b d -> (o p) b d"), att_sb[:, a])\
                    .then_inc(s_st[a], 16)

            def ahead(p, converting):
                for a in range(2):
                    s = 2 * p + a
                    for b in range(RB):
                        t = (4 * p + 4 + 2 * a + b) if converting else ((p + 1) & (SPH // 2 - 1)) * 4 + 2 * a + b
                        sp.wait_ge(s_msk, CPS * s + CPB * (b + 1))
                        if converting:
                            for hf in range(2):
                                sp.wait_ge(c.s_mask[hf], 16 * t + 16)
                        passed(sp, s_sp_passed)
                        load_mask(a, b, t)
                    sp.wait_ge(s_qk, CPS * (s + 1))
                    load_q(a, s + 2)
                    if a == 1 or not isinstance(p, int):
                        store(1 - a, s - 1)

            for a in range(2):
                load_q(a, a)
                for b in range(RB):
                    load_mask(a, b, 2 * a + b)
            ahead(0, True)
            with sp.Fori(1, SPH // 2 - 1) as p:
                ahead(p, True)
            with sp.Fori(SPH // 2 - 1, PAIRS - 1) as p:
                ahead(p, False)
            for s in range(STEPS - 3, STEPS):
                store(s % 2, s)
            for a in range(2):
                sp.wait_ge(s_st[a], 16 * (PAIRS + 1))

        @block.gpsimd
        def _(pool):
            with pool.Fori(PRE_MASKS, NB) as t:
                mask_block(pool, c, adj, mask_scr, t)
            for b in range(2):
                pool.wait_ge(c.s_mask[b], 16 * NB)
            with pool.Fori(1, H) as h:
                key_parts(pool, c, x2t, h, KC * h, free=CPS * SPH * h - CPB)
                value_parts(pool, c, v, h, KC * h, free=CPS * SPH * h - UPS)


def masked(dve, out, scores, mask, top):
    return dve.tensor_tensor_reduce(out=out, in0=scores, in1=mask, scale=1.0, scalar=LOWEST,
                                    op0=ALU.add, op1=ALU.max, accum_out=top)


def finished(p, i, back):
    q = i // CPS - back
    s = 2 * p + q
    return s, q % 2, not isinstance(p, int) or 0 <= s < STEPS


def step_count(p, i, lag):
    return 2 * p + (i - lag) // UPS + 1


def exp_count(p, i, lag, piece):
    return 2 * PIECES * (2 * p + (i - lag) // UPS) + PIECES + piece + 1


def aggregate(nc, ctx, x, adj, wnb_t, bnb, wline_t, bline, att_scr, acc_scr, out):
    y_hi = ctx.enter_context(nc.sbuf_tensor("y_hi", [P, NB, D], FR))
    y_lo = ctx.enter_context(nc.sbuf_tensor("y_lo", [P, NB, D], FR))
    with ExitStack() as phase:
        linear(nc, phase, x, wnb_t, wline_t, bline, att_scr, acc_scr, y_hi, y_lo)
    with ExitStack() as phase:
        neighbours(nc, phase, adj, bnb, acc_scr, y_hi, y_lo, out)


def linear(nc, ctx, x, wnb_t, wline_t, bline, att_scr, acc_scr, y_hi, y_lo):
    def sb(name, shape, dt=F32):
        return ctx.enter_context(nc.sbuf_tensor(name, shape, dt))

    def sem(name):
        return ctx.enter_context(nc.semaphore("s_l_" + name))

    KB = D // P
    R = 4
    x1 = sb("x1", [P, R, D])
    att = sb("att", [P, 2, H, DH])
    w_nb = sb("w_nb", [P, KB, D])
    w_line = sb("w_line", [P, KB, D])
    b_line = sb("b_line", [P, D])
    ident = sb("ident1", [P, P])
    stats = sb("stats1", [P, 2, 6])
    mv = sb("mv1", [P, 2, 2])
    ln = sb("ln1", [P, 2, 7])
    hn = sb("hn", [P, 2, D])
    ht = sb("ht", [P, 2, KB, P])
    lin = sb("lin", [P, 2, D])
    act_l = sb("act_l", [P, 2, D])
    psums = ctx.enter_context(nc.psum_tensor("pl", [P, 6, D], F32))
    p_t, p_y, p_l = (psums[:, 2 * k:2 * k + 2, :] for k in range(3))
    s_w, s_id, s_x1, s_bn, s_ag, s_var, s_std, s_ln, s_scale, s_h, s_t, s_ht, s_yl, s_yhi, s_ylo, s_lb, s_lk, s_acc = (
        sem(k) for k in ("w", "id", "x1", "bn", "ag", "var", "std", "ln", "scale", "h", "t", "ht", "yl", "yhi",
                         "ylo", "lb", "lk", "acc"))
    s_xld = [sem(f"xld{b}") for b in range(R)]
    s_passed = sem("dve_passed")
    s_ald = [sem(f"ald{b}") for b in range(2)]
    s_st = [sem(f"st{b}") for b in range(R)]
    LAST = 3

    def slots(eng, slot):
        for i in range(R):
            slot(i, i)
        with eng.Fori(1, NB // R) as p:
            for i in range(R):
                slot(R * p + i, i)
        for i in range(LAST):
            slot(NB + i, i)

    def has(t):
        return not isinstance(t, int) or 0 <= t < NB

    with nc.Block() as block:
        @block.sync
        def _(sp):
            att_rows = att_scr.rearrange("(h j) p b d -> j b p h d", h=H)
            x_rows = x.rearrange("(t p) c -> t p c", p=P)

            def load_x(t, r):
                sp.dma_start(x1[:, r, :], x_rows[bass.ds(t, 1)].rearrange("o p c -> (o p) c"))\
                    .then_inc(s_xld[r], 16)

            def load_att(j, b):
                sp.dma_start(att[:, b], att_rows[bass.ds(j, 1), b].rearrange("o p h d -> (o p) h d"))\
                    .then_inc(s_ald[b], 16)

            def store(t, r):
                sp.wait_ge(s_acc, t + 1)
                sp.dma_start(acc_scr[bass.ds(t, 1)].rearrange("o p c -> (o p) c"), x1[:, r, :])\
                    .then_inc(s_st[r], 16)

            for src, dst in ((wnb_t, w_nb), (wline_t, w_line)):
                sp.dma_start(dst[:, :, :], src.rearrange("(k p) c -> p k c", p=P)).then_inc(s_w, 16)
            sp.dma_start(b_line[:, :], bline).then_inc(s_w, 16)
            for i in range(2):
                load_x(i, i)
                load_att(0, i)
            for i in range(2, R):
                load_x(i, i)
                sp.wait_ge(s_x1, i - 1)
                load_att(1, i - 2)
            store(0, 0)
            with sp.Fori(1, NB // R) as p:
                for i in range(R):
                    t = R * p + i
                    sp.wait_ge(s_st[i], 16 * p)
                    load_x(t, i)
                    sp.wait_ge(s_x1, t - 1)
                    load_att(2 * p + i // 2, i % 2)
                    store(t - LAST, (i - LAST) % R)
            for t in range(NB - LAST, NB):
                store(t, t % R)
            for r in range(R):
                sp.wait_ge(s_st[r], 16 * (NB // R))

        @block.vector
        def _(dve):
            def slot(t, i):
                if has(t):
                    r, b = i % R, i % 2
                    dve.wait_ge(s_xld[r], 16 * ((t >> 2) + 1))
                    dve.wait_ge(s_ald[b], 16 * ((t >> 1) + 1))
                    dve.tensor_tensor(x1[:, r, :], x1[:, r, :], att[:, b].rearrange("p h d -> p (h d)"),
                                      ALU.add).then_inc(s_x1, 1)
                    dve.wait_ge(s_x1, t + 1)
                    dve.bn_stats(stats[:, b, :], x1[:, r, :]).then_inc(s_bn, 1)
                    dve.wait_ge(s_bn, t + 1)
                    passed(dve, s_passed)
                    dve.bn_aggr(mv[:, b, :], stats[:, b, :]).then_inc(s_ag, 1)
                    dve.wait_ge(s_ag, t + 1)
                    dve.tensor_scalar(ln[:, b, 0:1], mv[:, b, 1:2], EPS, None, ALU.add).then_inc(s_var, 1)
                u, r, b = t - 1, (i - 1) % R, (i - 1) % 2
                if has(u):
                    var, std, rstd, tmp, tmp2, scale, shift = (ln[:, b, k:k + 1] for k in range(7))
                    dve.wait_ge(s_std, u + 1)
                    refine_rstd(dve, var, std, rstd, tmp, tmp2, s_ln, 5 * u)
                    dve.scalar_tensor_tensor(shift, mv[:, b, 0:1], -1.0, rstd, ALU.mult, ALU.mult)\
                        .then_inc(s_scale, 1)
                u, r, b = t - LAST, (i - LAST) % R, (i - LAST) % 2
                if has(u):
                    dve.wait_ge(s_yhi, u + 1)
                    dve.tensor_tensor(y_lo[:, bass.ds(u, 1), :].rearrange("p o c -> p (o c)"), p_y[:, b, :],
                                      y_hi[:, bass.ds(u, 1), :].rearrange("p o c -> p (o c)").bitcast(F32),
                                      ALU.subtract).then_inc(s_ylo, 1)
                    dve.tensor_tensor(lin[:, b, :], p_l[:, b, :], b_line[:, :], ALU.add).then_inc(s_lb, 1)
                    dve.wait_ge(s_lb, u + 2)
                    dve.scalar_tensor_tensor(act_l[:, b, :], lin[:, b, :], 0.01, lin[:, b, :],
                                             ALU.mult, ALU.max).then_inc(s_lk, 1)
                    dve.wait_ge(s_lk, u + 1)
                    dve.tensor_tensor(x1[:, r, :], x1[:, r, :], act_l[:, b, :], ALU.add).then_inc(s_acc, 1)
            for s in (s_ylo, s_lb):
                dve.sem_inc(s, 1)
            dve.wait_ge(s_w, 48)
            slots(dve, slot)

        @block.scalar
        def _(act):
            def slot(t, i):
                b = i % 2
                if has(t):
                    act.wait_ge(s_var, t + 1)
                    act.activation(ln[:, b, 1:2], ln[:, b, 0:1], ACT.Sqrt).then_inc(s_std, 1)
                u, r, b = t - 1, (i - 1) % R, (i - 1) % 2
                if has(u):
                    act.wait_ge(s_scale, u + 1)
                    ge(act, s_t, u - 1)
                    act.activation(hn[:, b, :], x1[:, r, :], ACT.Relu, bias=ln[:, b, 6:7],
                                   scale=ln[:, b, 2:3]).then_inc(s_h, 1)
                u, b = t - 2, i % 2
                if has(u):
                    act.wait_ge(s_t, u + 1)
                    ge(act, s_yl, u - 1)
                    act.activation(ht[:, b], p_t[:, b, :].rearrange("p (k n) -> p k n", n=P), ACT.Copy)\
                        .then_inc(s_ht, 1)
                u, b = t - LAST, (i - LAST) % 2
                if has(u):
                    act.wait_ge(s_yl, u + 1)
                    act.activation(y_hi[:, bass.ds(u, 1), :].rearrange("p o c -> p (o c)"), p_y[:, b, :],
                                   ACT.Copy).then_inc(s_yhi, 1)
            slots(act, slot)

        @block.tensor
        def _(pe):
            def slot(t, i):
                u, b = t - 2, i % 2
                if has(u):
                    pe.wait_ge(s_h, u + 1)
                    ge(pe, s_ht, u - 1)
                    for k in range(KB):
                        last = pe.matmul(p_t[:, b, k * P:(k + 1) * P], hn[:, b, k * P:(k + 1) * P], ident[:, :],
                                         is_transpose=True, start=True, stop=True)
                    last.then_inc(s_t, 1)
                u, b = t - LAST, (i - LAST) % 2
                if has(u):
                    pe.wait_ge(s_ht, u + 1)
                    ge(pe, s_ylo, u)
                    ge(pe, s_lb, u)
                    for dst, w in ((p_y, w_nb), (p_l, w_line)):
                        for k in range(KB):
                            last = pe.matmul(dst[:, b, :], ht[:, b, k, :], w[:, k, :], start=k == 0,
                                             stop=k == KB - 1)
                    last.then_inc(s_yl, 1)
            pe.wait_ge(s_w, 48)
            pe.wait_ge(s_id, 2)
            slots(pe, slot)

        @block.gpsimd
        def _(pool):
            pool.memset(ident[:, :], 0.0).then_inc(s_id, 1)
            pool.wait_ge(s_id, 1)
            pool.affine_select(out=ident[:, :], in_=ident[:, :], compare_op=ALU.not_equal, fill=1.0,
                               base=0, pattern=[[-1, P]], channel_multiplier=1).then_inc(s_id, 1)


def neighbours(nc, ctx, adj, bnb, acc_scr, y_hi, y_lo, out):
    def sb(name, shape, dt=F32):
        return ctx.enter_context(nc.sbuf_tensor(name, shape, dt))

    def sem(name):
        return ctx.enter_context(nc.semaphore("s_n_" + name))

    G = 8
    NG = NB // G
    adj_i = sb("adj_i", [P, 2, N // 2], I32)
    edge = sb("edge", [P, 2, N], BF16)
    seen = sb("seen", [P, N], BF16)
    keep = sb("keep", [P, 2, N], BF16)
    keep_t = sb("keep_t", [P, 2, G, P], FR)
    ident = sb("identb", [P, P], BF16)
    b_nb = sb("b_nb", [P, D])
    count = sb("count", [P, 2, 3])
    acc = sb("acc", [P, 2, D])
    mean = sb("mean", [P, 2, D])
    leaky = sb("leaky", [P, 2, D])
    p_k = ctx.enter_context(nc.psum_tensor("p_k", [P, 2, G, P], BF16))
    p_o = ctx.enter_context(nc.psum_tensor("p_o", [P, 2, D], F32))
    s_id, s_b, s_edge, s_seen, s_cnt, s_rc, s_ind, s_keep, s_t, s_kt, s_grp, s_mean, s_leaky, s_out = (
        sem(k) for k in ("id", "b", "edge", "seen", "cnt", "rc", "ind", "keep", "t", "kt", "grp", "mean", "leaky",
                         "out"))
    s_adj = [sem(f"adj{b}") for b in range(2)]
    s_passed = sem("pool_passed")
    s_acc = [sem(f"acc{b}") for b in range(2)]
    s_st = [sem(f"st{b}") for b in range(2)]

    def slots(eng, slot):
        for i in range(2):
            slot(i, i, 0)
        with eng.Fori(1, NB // 2) as p:
            for i in range(2):
                slot(2 * p + i, i, p)
        for i in range(2):
            slot(NB + i, i, NB // 2)

    def has(t):
        return not isinstance(t, int) or 0 <= t < NB

    with nc.Block() as block:
        @block.sync
        def _(sp):
            for i in range(2):
                sp.sem_inc(s_st[i], 16)
            sp.dma_start(b_nb[:, :], bnb).then_inc(s_b, 16)

            def slot(t, i, p):
                if has(t):
                    w = N // 2
                    for hf in range(2):
                        ge(sp, s_edge, 2 * t + hf - 1)
                        sp.dma_start(adj_i[:, hf, :], adj[bass.ds(t * P, P), hf * w:(hf + 1) * w])\
                            .then_inc(s_adj[hf], 16)
                    ge(sp, s_out, t - 1)
                    sp.dma_start(acc[:, i, :], acc_scr[bass.ds(t, 1)].rearrange("o p c -> (o p) c"))\
                        .then_inc(s_acc[i], 16)
                u = t - 2
                if has(u):
                    sp.wait_ge(s_out, u + 1)
                    sp.dma_start(out[bass.ds(u * P, P), :], mean[:, i, :]).then_inc(s_st[i], 16)
            slots(sp, slot)
            for i in range(2):
                sp.wait_ge(s_st[i], 16 * (NB // 2 + 1))

        @block.gpsimd
        def _(pool):
            pool.memset(ident[:, :], 0.0).then_inc(s_id, 1)
            pool.wait_ge(s_id, 1)
            pool.affine_select(out=ident[:, :], in_=ident[:, :], compare_op=ALU.not_equal, fill=1.0,
                               base=0, pattern=[[-1, P]], channel_multiplier=1).then_inc(s_id, 1)
            w = N // 2

            def slot(t, i, p):
                if has(t):
                    ge(pool, s_keep, t - 1)
                    for hf in range(2):
                        pool.wait_ge(s_adj[hf], 16 * t + 16)
                        passed(pool, s_passed)
                        pool.tensor_scalar(edge[:, i, hf * w:(hf + 1) * w], adj_i[:, hf, :], 0, None, ALU.is_gt)\
                            .then_inc(s_edge, 1)
            slots(pool, slot)

        @block.vector
        def _(dve):
            def slot(t, i, p):
                u = t - 2
                if has(u):
                    dve.wait_ge(s_grp, NG * (u + 1))
                    ge(dve, s_st[i], 16 * p)
                    dve.scalar_tensor_tensor(mean[:, i, :], p_o[:, i, :], count[:, i, 1:2], b_nb[:, :],
                                             ALU.mult, ALU.add).then_inc(s_mean, 1)
                    dve.wait_ge(s_mean, u + 2)
                    dve.scalar_tensor_tensor(leaky[:, i, :], mean[:, i, :], 0.01, mean[:, i, :],
                                             ALU.mult, ALU.max).then_inc(s_leaky, 1)
                    dve.wait_ge(s_leaky, u + 1)
                    dve.wait_ge(s_acc[i], 16 * p)
                    dve.scalar_tensor_tensor(mean[:, i, :], leaky[:, i, :], count[:, i, 2:3], acc[:, i, :],
                                             ALU.mult, ALU.add).then_inc(s_out, 1)
                if has(t):
                    dve.wait_ge(s_edge, 2 * t + 2)
                    dve.tensor_tensor_scan(seen[:, :], edge[:, i, :], edge[:, i, :], 0.0, ALU.add, ALU.max)\
                        .then_inc(s_seen, 1)
                    dve.wait_ge(s_seen, t + 1)
                    ge(dve, s_t, NG * (t - 1))
                    dve.scalar_tensor_tensor(keep[:, i, :], seen[:, :], float(KEEP), edge[:, i, :],
                                             ALU.is_le, ALU.mult).then_inc(s_keep, 1)
                    if isinstance(t, int) and t < 2:
                        pass
                    else:
                        dve.wait_ge(s_out, t - 1)
                    dve.tensor_scalar(count[:, i, 0:1], seen[:, N - 1:N], float(KEEP), 1.0, ALU.min, ALU.max)\
                        .then_inc(s_cnt, 1)
                    dve.tensor_scalar(count[:, i, 2:3], seen[:, N - 1:N], 1.0, None, ALU.min).then_inc(s_ind, 1)
                    dve.wait_ge(s_cnt, t + 1)
                    dve.reciprocal(count[:, i, 1:2], count[:, i, 0:1]).then_inc(s_rc, 1)
                    dve.wait_ge(s_rc, t + 1)
                    dve.wait_ge(s_ind, t + 1)
                    dve.wait_ge(s_keep, t + 1)
            dve.sem_inc(s_mean, 1)
            dve.wait_ge(s_b, 16)
            slots(dve, slot)

        @block.scalar
        def _(act):
            def slot(t, i, p):
                u = t - 1
                if has(u):
                    for g in range(NG):
                        n = NG * u + g
                        act.wait_ge(s_t, n + 1)
                        ge(act, s_grp, n - 1)
                        act.activation(keep_t[:, g % 2], p_k[:, g % 2], ACT.Copy).then_inc(s_kt, 1)
            slots(act, slot)

        @block.tensor
        def _(pe):
            def transposes(u, i, g):
                n = NG * u + g
                if g == 0:
                    pe.wait_ge(s_keep, u + 1)
                ge(pe, s_kt, n - 1)
                for m in range(G):
                    last = pe.matmul(p_k[:, g % 2, m, :], keep[:, i, (G * g + m) * P:(G * g + m + 1) * P],
                                     ident[:, :], is_transpose=True, start=True, stop=True)
                last.then_inc(s_t, 1)

            def products(u, i, g):
                n = NG * u + g
                if g == 0:
                    ge(pe, s_mean, u)
                pe.wait_ge(s_kt, n + 1)
                for m in range(G):
                    for s, y in enumerate((y_hi, y_lo)):
                        last = pe.matmul(p_o[:, i, :], keep_t[:, g % 2, m, :], y[:, G * g + m, :],
                                         start=(g == 0 and m == 0 and s == 0),
                                         stop=(g == NG - 1 and m == G - 1 and s == 1))
                    if m == G - 1:
                        last.then_inc(s_grp, 1)

            def slot(t, i, p):
                u, a = t - 1, (i - 1) % 2
                if has(u):
                    for g in range(NG):
                        transposes(u, a, g)
                        if g > 0:
                            products(u, a, g - 1)
                    products(u, a, NG - 1)
            pe.wait_ge(s_id, 2)
            slots(pe, slot)


_INS = ["x", "adj", "x2t", "v", "wnb_t", "bnb", "wline_t", "bline"]


def kernel(x, adj, L0_gnn_x2, L0_gnn_v, L1_gnn_W_nb, L1_gnn_b_nb, L1_gnn_W_line, L1_gnn_b_line):
    import concourse.bacc as bacc
    from concourse.bass_utils import run_bass_kernel_spmd

    laid = dict(
        x=x, adj=adj, x2t=np.asarray(L0_gnn_x2).T, v=L0_gnn_v,
        wnb_t=np.asarray(L1_gnn_W_nb).T, bnb=np.broadcast_to(np.asarray(L1_gnn_b_nb), (P, D)),
        wline_t=np.asarray(L1_gnn_W_line).T, bline=np.broadcast_to(np.asarray(L1_gnn_b_line), (P, D)),
    )
    nc = bacc.Bacc("TRN2", target_bir_lowering=False, num_devices=1)
    arrays, args = {}, []
    for name in _INS:
        a = np.ascontiguousarray(laid[name])
        arrays[f"in_{name}"] = a
        args.append(nc.dram_tensor(f"in_{name}", a.shape, mybir.dt.from_np(a.dtype), kind="ExternalInput").ap())
    out = nc.dram_tensor("out", (N, D), F32, kind="ExternalOutput").ap()
    build(nc, *args, out)
    r = run_bass_kernel_spmd(nc, [arrays], core_ids=[0])
    return r.results[0]["out"]
```
